# Optimizing a Trainium2 kernel written in Bass

```python
import numpy as np
import jax
import jax.numpy as jnp

def _softmax(x, axis=-1):
    return jax.nn.softmax(x, axis=axis)

def _gelu(x):
    return jax.nn.gelu(x, approximate=True)

def _silu(x):
    return jax.nn.silu(x)

def _sigmoid(x):
    return jax.nn.sigmoid(x)

def _layernorm(x, axis=-1, eps=1e-05):
    m = jnp.mean(x, axis=axis, keepdims=True)
    v = jnp.var(x, axis=axis, keepdims=True)
    return (x - m) / jnp.sqrt(v + eps)

def _scatter_add(tgt, idx, src, axis=0):
    return tgt.at[idx].add(src)

def _segment_sum(src, seg, n):
    return jax.ops.segment_sum(src, seg, n)
kernel_name = 'mk_dlrm_tower_d1_rec_r8_af06ba'

def setup_inputs(seed: int=0):
    np.random.seed(seed)
    _w = jnp.asarray

    def _rec_inputs():
        import jax
        import jax.numpy as jnp
        _tk = jax.random.key(seed)
        ids = jnp.stack([jax.random.randint(jax.random.fold_in(_tk, 200 + f), (512,), 0, v, jnp.int32) for f, v in enumerate([12500, 12500, 1000, 1000, 12500, 1000, 1000, 125000, 1250, 1000, 1000, 1250, 1000, 1000, 1250, 1000, 12500, 12500, 1000, 1000, 12500, 12500, 1250, 12500, 1250, 1000])], axis=1)
        tbl_0 = 0.05 * jax.random.normal(jax.random.fold_in(_tk, 500 + 0), (12500, 128), jnp.float32)
        tbl_1 = 0.05 * jax.random.normal(jax.random.fold_in(_tk, 500 + 1), (12500, 128), jnp.float32)
        tbl_2 = 0.05 * jax.random.normal(jax.random.fold_in(_tk, 500 + 2), (1000, 128), jnp.float32)
        tbl_3 = 0.05 * jax.random.normal(jax.random.fold_in(_tk, 500 + 3), (1000, 128), jnp.float32)
        tbl_4 = 0.05 * jax.random.normal(jax.random.fold_in(_tk, 500 + 4), (12500, 128), jnp.float32)
        tbl_5 = 0.05 * jax.random.normal(jax.random.fold_in(_tk, 500 + 5), (1000, 128), jnp.float32)
        tbl_6 = 0.05 * jax.random.normal(jax.random.fold_in(_tk, 500 + 6), (1000, 128), jnp.float32)
        tbl_7 = 0.05 * jax.random.normal(jax.random.fold_in(_tk, 500 + 7), (125000, 128), jnp.float32)
        tbl_8 = 0.05 * jax.random.normal(jax.random.fold_in(_tk, 500 + 8), (1250, 128), jnp.float32)
        tbl_9 = 0.05 * jax.random.normal(jax.random.fold_in(_tk, 500 + 9), (1000, 128), jnp.float32)
        tbl_10 = 0.05 * jax.random.normal(jax.random.fold_in(_tk, 500 + 10), (1000, 128), jnp.float32)
        tbl_11 = 0.05 * jax.random.normal(jax.random.fold_in(_tk, 500 + 11), (1250, 128), jnp.float32)
        tbl_12 = 0.05 * jax.random.normal(jax.random.fold_in(_tk, 500 + 12), (1000, 128), jnp.float32)
        tbl_13 = 0.05 * jax.random.normal(jax.random.fold_in(_tk, 500 + 13), (1000, 128), jnp.float32)
        tbl_14 = 0.05 * jax.random.normal(jax.random.fold_in(_tk, 500 + 14), (1250, 128), jnp.float32)
        tbl_15 = 0.05 * jax.random.normal(jax.random.fold_in(_tk, 500 + 15), (1000, 128), jnp.float32)
        tbl_16 = 0.05 * jax.random.normal(jax.random.fold_in(_tk, 500 + 16), (12500, 128), jnp.float32)
        tbl_17 = 0.05 * jax.random.normal(jax.random.fold_in(_tk, 500 + 17), (12500, 128), jnp.float32)
        tbl_18 = 0.05 * jax.random.normal(jax.random.fold_in(_tk, 500 + 18), (1000, 128), jnp.float32)
        tbl_19 = 0.05 * jax.random.normal(jax.random.fold_in(_tk, 500 + 19), (1000, 128), jnp.float32)
        tbl_20 = 0.05 * jax.random.normal(jax.random.fold_in(_tk, 500 + 20), (12500, 128), jnp.float32)
        tbl_21 = 0.05 * jax.random.normal(jax.random.fold_in(_tk, 500 + 21), (12500, 128), jnp.float32)
        tbl_22 = 0.05 * jax.random.normal(jax.random.fold_in(_tk, 500 + 22), (1250, 128), jnp.float32)
        tbl_23 = 0.05 * jax.random.normal(jax.random.fold_in(_tk, 500 + 23), (12500, 128), jnp.float32)
        tbl_24 = 0.05 * jax.random.normal(jax.random.fold_in(_tk, 500 + 24), (1250, 128), jnp.float32)
        tbl_25 = 0.05 * jax.random.normal(jax.random.fold_in(_tk, 500 + 25), (1000, 128), jnp.float32)
        _rk = jax.random.fold_in(_tk, 7)
        r_dense_features = -0.000520686 + 1.00062 * jax.random.normal(jax.random.fold_in(_rk, 101), (512, 128), jnp.float32)
        W_top1 = 0.0405887 * jax.random.normal(jax.random.fold_in(_tk, 801), (607, 512), jnp.float32)
        W_top2 = 0.0441942 * jax.random.normal(jax.random.fold_in(_tk, 802), (512, 256), jnp.float32)
        W_top3 = 0.0625 * jax.random.normal(jax.random.fold_in(_tk, 803), (256, 1), jnp.float32)
        b_top1 = jnp.zeros((512,), jnp.float32)
        b_top2 = jnp.zeros((256,), jnp.float32)
        return (r_dense_features, ids, tbl_0, tbl_1, tbl_2, tbl_3, tbl_4, tbl_5, tbl_6, tbl_7, tbl_8, tbl_9, tbl_10, tbl_11, tbl_12, tbl_13, tbl_14, tbl_15, tbl_16, tbl_17, tbl_18, tbl_19, tbl_20, tbl_21, tbl_22, tbl_23, tbl_24, tbl_25, W_top1, b_top1, W_top2, b_top2, W_top3)
    r_dense_features, ids, tbl_0, tbl_1, tbl_2, tbl_3, tbl_4, tbl_5, tbl_6, tbl_7, tbl_8, tbl_9, tbl_10, tbl_11, tbl_12, tbl_13, tbl_14, tbl_15, tbl_16, tbl_17, tbl_18, tbl_19, tbl_20, tbl_21, tbl_22, tbl_23, tbl_24, tbl_25, W_top1, b_top1, W_top2, b_top2, W_top3 = _rec_inputs()

    def _L0_rec_setup():
        import jax, jax.numpy as jnp
        import numpy as np
        B, F, D = (2048, 26, 128)
        key = jax.random.key(seed)
        k1, k2 = jax.random.split(key)
        dense_features = jax.random.normal(k1, (B, D), dtype=jnp.float32)
        sparse_values = jax.random.normal(k2, (B, F, D), dtype=jnp.float32)
        return {'dense_features': dense_features, 'sparse_values': sparse_values}
    _L0_rec_all = _L0_rec_setup()
    _L0_rec_in = {k: v for k, v in _L0_rec_all.items() if k in ()}
    del _L0_rec_all
    return {'r_dense_features': r_dense_features, 'ids': ids, 'tbl_0': tbl_0, 'tbl_1': tbl_1, 'tbl_2': tbl_2, 'tbl_3': tbl_3, 'tbl_4': tbl_4, 'tbl_5': tbl_5, 'tbl_6': tbl_6, 'tbl_7': tbl_7, 'tbl_8': tbl_8, 'tbl_9': tbl_9, 'tbl_10': tbl_10, 'tbl_11': tbl_11, 'tbl_12': tbl_12, 'tbl_13': tbl_13, 'tbl_14': tbl_14, 'tbl_15': tbl_15, 'tbl_16': tbl_16, 'tbl_17': tbl_17, 'tbl_18': tbl_18, 'tbl_19': tbl_19, 'tbl_20': tbl_20, 'tbl_21': tbl_21, 'tbl_22': tbl_22, 'tbl_23': tbl_23, 'tbl_24': tbl_24, 'tbl_25': tbl_25, 'W_top1': W_top1, 'b_top1': b_top1, 'W_top2': W_top2, 'b_top2': b_top2, 'W_top3': W_top3}

def reference(r_dense_features, ids, tbl_0, tbl_1, tbl_2, tbl_3, tbl_4, tbl_5, tbl_6, tbl_7, tbl_8, tbl_9, tbl_10, tbl_11, tbl_12, tbl_13, tbl_14, tbl_15, tbl_16, tbl_17, tbl_18, tbl_19, tbl_20, tbl_21, tbl_22, tbl_23, tbl_24, tbl_25, W_top1, b_top1, W_top2, b_top2, W_top3):
    import jax
    import jax.numpy as jnp

    def _L0_rec_ref(dense_features, sparse_values):
        import jax, jax.numpy as jnp
        import numpy as np
        B, F, D = (2048, 26, 128)
        sd = jnp.einsum('bfd,bd->bf', sparse_values, dense_features)
        ss = jnp.einsum('bfd,bgd->bfg', sparse_values, sparse_values)
        iu, ju = jnp.triu_indices(F, k=1)
        pairs = ss[:, iu, ju]
        return jnp.concatenate([dense_features, sd, pairs], axis=1)
    e = jnp.stack([tbl_0[ids[:, 0]], tbl_1[ids[:, 1]], tbl_2[ids[:, 2]], tbl_3[ids[:, 3]], tbl_4[ids[:, 4]], tbl_5[ids[:, 5]], tbl_6[ids[:, 6]], tbl_7[ids[:, 7]], tbl_8[ids[:, 8]], tbl_9[ids[:, 9]], tbl_10[ids[:, 10]], tbl_11[ids[:, 11]], tbl_12[ids[:, 12]], tbl_13[ids[:, 13]], tbl_14[ids[:, 14]], tbl_15[ids[:, 15]], tbl_16[ids[:, 16]], tbl_17[ids[:, 17]], tbl_18[ids[:, 18]], tbl_19[ids[:, 19]], tbl_20[ids[:, 20]], tbl_21[ids[:, 21]], tbl_22[ids[:, 22]], tbl_23[ids[:, 23]], tbl_24[ids[:, 24]], tbl_25[ids[:, 25]]], axis=1)
    z = _L0_rec_ref(r_dense_features, e)
    z = z.reshape(z.shape[0], -1)
    h = jnp.concatenate([z, r_dense_features], axis=1)
    h = jnp.maximum(h @ W_top1 + b_top1, 0.0)
    h = jnp.maximum(h @ W_top2 + b_top2, 0.0)
    y = h @ W_top3
    return y

_drawn_inputs = setup_inputs


def setup_inputs(seed=0):
    import zlib

    import numpy as np

    out = dict(_drawn_inputs(seed))
    spreads = {'b_top1': (0.0, 0.1), 'b_top2': (0.0, 0.1)}
    factors = {}
    for name, (base, spread) in spreads.items():
        noise = np.random.default_rng([zlib.crc32(name.encode()), seed]).standard_normal(out[name].shape)
        drawn = base * np.exp(spread * noise) if base else spread * noise
        out[name] = jnp.asarray(drawn.astype(out[name].dtype))
    for name, factor in factors.items():
        out[name] = (out[name] * factor).astype(out[name].dtype)
    return out
```

```python
from contextlib import ExitStack

import concourse.bass as bass
from concourse import mybir

F32 = mybir.dt.float32
I32 = mybir.dt.int32
ALU = mybir.AluOpType
ACT = mybir.ActivationFunctionType

P = 128
SLOTS = 27
PAD = 32
SPG = P // PAD
GROUPS = P // SPG
BATCH = 4
BANK = 512
GPB = 4
UNIT = 2 * GPB
SPAN = SLOTS // 2 + 1
PAIRS = SLOTS * (SLOTS - 1) // 2
PAIR_TILES = [(a, min(a + P, PAIRS)) for a in range(0, PAIRS, P)]
LOOKUPS = 4
AHEAD = (2, 1, 1, 1)


def look_rows(vocabulary):
    return max(n for n in range(1, P + 1) if vocabulary % n == 0)


def batches(looked, gathered):
    look = [list(range(a, min(a + 2, looked))) for a in range(0, looked - looked % 2, 2)]
    look += [[i] for i in range(looked - looked % 2, looked)]
    gather = [list(range(a, min(a + BATCH, gathered))) for a in range(0, gathered, BATCH)]
    order = []
    while look or gather:
        order += [(True, b) for b in look[:1]] + [(False, b) for b in gather[:1 if look[1:] else BATCH]]
        look, gather = look[1:], gather[1 if look[1:] else BATCH:]
    return order


def pair_rows(dense_dim, order):
    def row(a, b):
        return dense_dim + a * (SLOTS - 1) - a * (a - 1) // 2 + b - a - 1

    feature = [0] + [f + 1 for f in order]
    rows = []
    for k in range(1, SPAN + 1):
        for c in range(SLOTS - 1):
            rows.append(row(*sorted(feature[s] for s in divmod(c * SLOTS + c + k, SLOTS))))
    return rows[:PAIRS]


def dlrm_tower(nc, dense, gather_ids, look_ids, gather_tables, look_tables,
               w_dense_a, w_pairs, w_dense_b, w2, columns, out):
    B, D = dense.shape
    F, L = len(gather_tables), len(look_tables)
    TILES = B // P
    N1, N2 = w2.shape
    C1, C2 = N1 // P, N2 // P
    LP = look_rows(look_tables[0].shape[0])
    LC = look_tables[0].shape[0] // LP
    BATCHES = batches(L, F)
    NB = len(BATCHES)
    UNITS = GROUPS // UNIT
    assert D == P and L + F == SLOTS - 1

    with ExitStack() as ctx:
        def sb(name, shape, dt=F32):
            return ctx.enter_context(nc.sbuf_tensor(name, shape, dt))

        def psum(name, shape):
            return ctx.enter_context(nc.psum_tensor(name, shape, F32))

        def sem(name):
            return ctx.enter_context(nc.semaphore(name))

        ids_sb = sb("ids_sb", [P, TILES, F], I32)
        look_ids_sb = sb("look_ids_sb", [P, L, B], I32)
        look_sb = sb("look_sb", [LP, L, LC, D])
        row_of = sb("row_of", [LP, LC])
        one_hot = sb("one_hot", [LP, L, LC, B])
        dense_sb = sb("dense_sb", [P, TILES, D])
        dense_t = sb("dense_t", [P, B])
        rows = sb("rows", [P, F, D])
        feats = sb("feats", [P, GROUPS, SPG, PAD])
        gram_sb = sb("gram_sb", [P, SLOTS, GROUPS])
        dots_pad = sb("dots_pad", [P, SLOTS + 1, PAD])
        dots = sb("dots", [P, (SLOTS + 1) * SLOTS])
        pairs = sb("pairs", [P, SPAN * (SLOTS - 1)])
        pairs_t = sb("pairs_t", [P, len(PAIR_TILES), P])
        h1_dense = sb("h1_dense", [P, C1, B])
        h1_sum = sb("h1_sum", [P, C1, P])
        h1 = sb("h1", [P, C1, P])
        h2 = sb("h2", [P, C2, P])
        y = sb("y", [1, B])
        ident = sb("ident", [P, P])
        wd_sb = sb("wd_sb", [P, 2, N1])
        wp_sb = sb("wp_sb", [P, len(PAIR_TILES), N1])
        w2_sb = sb("w2_sb", [P, C1, N2])
        columns_sb = sb("columns_sb", [P, C1 + 2 * C2])
        b1_sb, b2_sb, w3_sb = (columns_sb[:, a:b] for a, b in ((0, C1), (C1, C1 + C2), (C1 + C2, C1 + 2 * C2)))

        turn_ps = psum("turn_ps", [P, 2, BATCH, P])
        gram_ps = psum("gram_ps", [P, 2 * UNIT // GPB, BANK])
        pair_ps = psum("pair_ps", [P, BANK])
        l23_ps = psum("l23_ps", [P, BANK])

        def h1_ps(c):
            return gram_ps[:, c, 0:P]

        def h2_ps(m):
            return (pair_ps if m == 0 else l23_ps)[:, 0:P]

        assert C1 == 2 * UNIT // GPB and C2 == 2
        y_ps = l23_ps[0:1, P:2 * P]

        ids_loaded = sem("ids_loaded")
        look_ids_loaded = [sem(f"look_ids_loaded_{i}") for i in range(L)]
        dense_loaded = sem("dense_loaded")
        look_loaded = [sem(f"look_loaded_{i}") for i in range(L)]
        dense_weights_loaded = sem("dense_weights_loaded")
        columns_loaded = sem("columns_loaded")
        weights_loaded = sem("weights_loaded")
        gathered = [sem(f"gathered_{f}") for f in range(F)]
        zeroed = sem("zeroed")
        ident_made = sem("ident_made")
        rows_numbered = sem("rows_numbered")
        pads_zeroed = sem("pads_zeroed")
        dense_turned = sem("dense_turned")
        dense_kept = sem("dense_kept")
        dense_placed = sem("dense_placed")
        hot_made = sem("hot_made")
        turned = sem("turned")
        kept = sem("kept")
        gram_done = sem("gram_done")
        drawn_dve = sem("drawn_dve")
        drawn_act = sem("drawn_act")
        dots_turned = sem("dots_turned")
        dots_packed = sem("dots_packed")
        pairs_packed = sem("pairs_packed")
        pairs_turned = sem("pairs_turned")
        pairs_kept = sem("pairs_kept")
        l1_dense_done = sem("l1_dense_done")
        h1_dense_kept = sem("h1_dense_kept")
        l1_done = sem("l1_done")
        h1_summed = sem("h1_summed")
        h1_kept = sem("h1_kept")
        l2_done = sem("l2_done")
        h2_kept = sem("h2_kept")
        l3_done = sem("l3_done")
        y_kept = sem("y_kept")
        y_stored = sem("y_stored")

        def keep_batch(copy, j):
            looked, which = BATCHES[j]
            first = 1 + which[0] + (0 if looked else L)
            src = turn_ps[:, j % 2, 0:len(which), :].rearrange("p f (s q) -> p s q f", s=SPG)
            return copy(feats[:, :, :, first:first + len(which)].rearrange("p q s f -> p s q f"), src)

        def draw_block(copy, u, s):
            at = slice(s * PAD, (s + 1) * PAD)
            bank = (u % 2) * (UNIT // GPB)
            src = gram_ps[at, bank:bank + UNIT // GPB, 0:GPB * SPG * SLOTS].rearrange(
                "p h (l s c) -> p h l s c", l=GPB, s=SPG)[:, :, :, s, :]
            dst = gram_sb[at, :, u * UNIT:(u + 1) * UNIT].rearrange("p c (h l) -> p h l c", l=GPB)
            return copy(dst, src)

        block = ctx.enter_context(nc.Block())

        @block.sync
        def _(sp):
            sp.dma_start(ids_sb[:], gather_ids.rearrange("(t p) f -> p t f", p=P)).then_inc(ids_loaded, 16)
            sp.dma_start(dense_sb[:], dense.rearrange("(t p) d -> p t d", p=P)).then_inc(dense_loaded, 16)
            for i in range(L):
                sp.dma_start(look_ids_sb[:, i, :], look_ids[i].partition_broadcast(P)).then_inc(look_ids_loaded[i], 16)
            sp.dma_start(wd_sb[:, 0, :], w_dense_a).then_inc(dense_weights_loaded, 16)
            sp.dma_start(wd_sb[:, 1, :], w_dense_b).then_inc(dense_weights_loaded, 16)
            sp.dma_start(columns_sb[:], columns).then_inc(columns_loaded, 16)
            for i in range(L):
                sp.dma_start(look_sb[:, i, :, :].rearrange("p k d -> p (k d)"),
                             look_tables[i].rearrange("(p k) d -> p (k d)", k=LC)).then_inc(look_loaded[i], 16)
            for i, (a, b) in enumerate(PAIR_TILES):
                sp.dma_start(wp_sb[0:b - a, i, :], w_pairs[a:b, :]).then_inc(weights_loaded, 16)
            sp.dma_start(w2_sb[:], w2.rearrange("(c p) n -> p c n", p=P)).then_inc(weights_loaded, 16)
            sp.wait_ge(y_kept, TILES)
            sp.dma_start(out.rearrange("b o -> o b"), y[:]).then_inc(y_stored, 16)
            sp.wait_ge(y_stored, 16)

        WEIGHTS = 16 * (1 + len(PAIR_TILES))

        @block.gpsimd
        def _(pool):
            nc.gpsimd.memset(ident[:], 0.0).then_inc(zeroed, 1)
            nc.gpsimd.iota(row_of[:], [[1, LC]], base=0, channel_multiplier=LC,
                           allow_small_or_imprecise_dtypes=True).then_inc(rows_numbered, 1)
            pool.wait_ge(zeroed, 1)
            nc.gpsimd.affine_select(out=ident[:], in_=ident[:], compare_op=ALU.not_equal, fill=1.0, base=0,
                                    pattern=[[-1, P]], channel_multiplier=1).then_inc(ident_made, 1)
            pool.wait_ge(ids_loaded, 16)
            for t in range(TILES):
                for j, (looked, which) in enumerate(BATCHES):
                    if looked:
                        continue
                    if t >= 1:
                        pool.wait_ge(turned, (t - 1) * NB + j + 1)
                    for f in which:
                        nc.gpsimd.indirect_dma_start(
                            out=rows[:, f, :], out_offset=None, in_=gather_tables[f],
                            in_offset=bass.IndirectOffsetOnAxis(ap=ids_sb[:, t, f:f + 1], axis=0)
                        ).then_inc(gathered[f], 16)

        @block.tensor
        def _(pe):
            def turn(t, j, first=False):
                if j >= 2:
                    pe.wait_ge(kept, t * NB + j - 1)
                looked, which = BATCHES[j]
                for at, f in enumerate(which):
                    if looked:
                        if first:
                            pe.wait_ge(look_loaded[f], 16)
                            pe.wait_ge(hot_made, f + 1)
                        for k in range(LC):
                            last = nc.tensor.matmul(turn_ps[:, j % 2, at, :], look_sb[:, f, k, :],
                                                    one_hot[:, f, k, bass.ds(t * P, P)],
                                                    start=(k == 0), stop=(k == LC - 1))
                    else:
                        pe.wait_ge(gathered[f], (t + 1) * 16)
                        last = nc.tensor.transpose(turn_ps[:, j % 2, at, :], rows[:, f, :], ident[:])
                last.then_inc(turned, 1)

            def gram(t):
                pe.wait_ge(kept, (t + 1) * NB)
                pe.wait_ge(dense_placed, t + 1)
                for u in range(UNITS):
                    if u >= 2:
                        pe.wait_ge(drawn_dve, t * UNITS + u - 1)
                        pe.wait_ge(drawn_act, t * UNITS + u - 1)
                    for i in range(UNIT):
                        q = u * UNIT + i
                        at = i % GPB * SPG * SLOTS
                        dst = gram_ps[:, (u % 2) * (UNIT // GPB) + i // GPB, at:at + SPG * SLOTS]
                        last = nc.tensor.matmul(dst.rearrange("p (s c) -> p s c", s=SPG),
                                                feats[:, q, :, :].rearrange("p s c -> p (s c)"),
                                                feats[:, q, :, 0:SLOTS], start=True, stop=True)
                    last.then_inc(gram_done, 1)

            def layer1_dense(c):
                for half in range(2):
                    last = nc.tensor.matmul(gram_ps[:, c, 0:B], wd_sb[:, half, c * P:(c + 1) * P], dense_t[:],
                                            start=(half == 0), stop=(half == 1))
                last.then_inc(l1_dense_done, 1)

            def turn_pairs(t):
                pe.wait_ge(pairs_packed, t + 1)
                for i, (a, b) in enumerate(PAIR_TILES):
                    last = nc.tensor.transpose(pair_ps[0:b - a, i * P:(i + 1) * P], pairs[:, a:b], ident[:])
                last.then_inc(pairs_turned, 1)

            def layer1_pairs(t):
                for c in range(C1):
                    for i, (a, b) in enumerate(PAIR_TILES):
                        pe.wait_ge(pairs_kept, t * 2 + (1 if b - a == P else 2))
                        last = nc.tensor.matmul(h1_ps(c), wp_sb[0:b - a, i, c * P:(c + 1) * P],
                                                pairs_t[0:b - a, i, :], start=(i == 0),
                                                stop=(i == len(PAIR_TILES) - 1))
                    last.then_inc(l1_done, 1)

            def layer2(t):
                for c in range(C1):
                    pe.wait_ge(h1_kept, t * C1 + c + 1)
                    for m in range(C2):
                        last = nc.tensor.matmul(h2_ps(m), w2_sb[:, c, m * P:(m + 1) * P], h1[:, c, :],
                                                start=(c == 0), stop=(c == C1 - 1))
                        if c == C1 - 1:
                            last.then_inc(l2_done, 1)

            def layer3(t):
                pe.wait_ge(h2_kept, (t + 1) * C2)
                for m in range(C2):
                    last = nc.tensor.matmul(y_ps, w3_sb[:, m:m + 1], h2[:, m, :], start=(m == 0), stop=(m == C2 - 1))
                last.then_inc(l3_done, 1)

            def tile(t, ahead):
                gram(t)
                todo = list(range(NB)) if ahead else []
                for step, share in ((turn_pairs, AHEAD[0]), (layer1_pairs, AHEAD[1]), (layer2, AHEAD[2]),
                                    (layer3, AHEAD[3])):
                    for j in todo[:share]:
                        turn(t + 1, j)
                    todo = todo[share:]
                    step(t)
                for j in todo:
                    turn(t + 1, j)

            pe.wait_ge(ident_made, 1)
            pe.wait_ge(dense_loaded, 16)
            for t in range(TILES):
                last = nc.tensor.transpose(turn_ps[:, 1, t, :], dense_sb[:, t, :], ident[:])
            last.then_inc(dense_turned, 1)
            pe.wait_ge(dense_kept, 1)
            pe.wait_ge(dense_weights_loaded, 32)
            for c in range(C1):
                layer1_dense(c)
            for j in range(NB):
                turn(0, j, first=True)
            pe.wait_ge(weights_loaded, WEIGHTS)
            pe.wait_ge(h1_dense_kept, C1)
            with pe.Fori(0, TILES - 1) as t:
                tile(t, True)
            tile(TILES - 1, False)

        @block.vector
        def _(dve):
            def make_hot(i):
                for k in range(LC):
                    last = nc.vector.tensor_scalar(one_hot[:, i, k, :], look_ids_sb[0:LP, i, :],
                                                   row_of[:, k:k + 1], None, ALU.is_equal)
                last.then_inc(hot_made, 1)

            def tile(t):
                for u in range(UNITS):
                    dve.wait_ge(gram_done, t * UNITS + u + 1)
                    draw_block(nc.vector.tensor_copy, u, 0)
                    draw_block(nc.vector.tensor_copy, u, 1).then_inc(drawn_dve, 1)
                dve.wait_ge(drawn_dve, (t + 1) * UNITS)
                dve.wait_ge(drawn_act, (t + 1) * UNITS)
                nc.vector.transpose(dots_pad[:, 0:SLOTS, :].rearrange("p c f -> p (c f)"),
                                    gram_sb[:].rearrange("p c q -> p (c q)")).then_inc(dots_turned, 1)
                dve.wait_ge(dots_turned, t + 1)
                nc.vector.tensor_copy(dots[:].rearrange("p (c f) -> p c f", f=SLOTS),
                                      dots_pad[:, :, 0:SLOTS]).then_inc(dots_packed, 1)
                dve.wait_ge(dots_packed, t + 1)
                nc.vector.tensor_copy(pairs[:].rearrange("p (k c) -> p k c", k=SPAN),
                                      dots[:, 1:1 + (SLOTS - 1) * (SLOTS + 1)].rearrange(
                                          "p (c k) -> p k c", k=SLOTS + 1)[:, 0:SPAN, :]).then_inc(pairs_packed, 1)
                dve.wait_ge(pairs_turned, t + 1)
                whole = PAIRS // P
                nc.vector.tensor_copy(pairs_t[:, 0:whole, :],
                                      pair_ps[:, 0:whole * P].rearrange("p (i b) -> p i b", b=P)
                                      ).then_inc(pairs_kept, 1)
                rest = PAIRS - whole * P
                nc.vector.tensor_copy(pairs_t[0:rest, whole, :], pair_ps[0:rest, whole * P:(whole + 1) * P]
                                      ).then_inc(pairs_kept, 1)
                for c in range(C1):
                    dve.wait_ge(l1_done, t * C1 + c + 1)
                    nc.vector.tensor_tensor(h1_sum[:, c, :], h1_ps(c), h1_dense[:, c, bass.ds(t * P, P)],
                                            ALU.add).then_inc(h1_summed, 1)
                for m in range(C2):
                    dve.wait_ge(l2_done, t * C2 + m + 1)
                    nc.vector.tensor_scalar(h2[:, m, :], h2_ps(m), b2_sb[:, m:m + 1], 0.0,
                                            ALU.add, ALU.max).then_inc(h2_kept, 1)
                dve.wait_ge(l3_done, t + 1)
                nc.vector.tensor_copy(y[:, bass.ds(t * P, P)], y_ps).then_inc(y_kept, 1)

            nc.vector.memset(feats[:, :, :, SLOTS:PAD], 0.0).then_inc(pads_zeroed, 1)
            nc.vector.memset(dots_pad[:, SLOTS, :], 0.0).then_inc(pads_zeroed, 1)
            dve.wait_ge(pads_zeroed, 2)
            dve.wait_ge(dense_turned, 1)
            nc.vector.tensor_copy(dense_t[:].rearrange("p (t b) -> p t b", b=P), turn_ps[:, 1, :, :]).then_inc(dense_kept, 1)
            dve.wait_ge(rows_numbered, 1)
            for i in range(L):
                dve.wait_ge(look_ids_loaded[i], 16)
                make_hot(i)
            dve.wait_ge(h1_dense_kept, C1)
            with dve.Fori(0, TILES - 1) as t:
                tile(t)
            tile(TILES - 1)

        @block.scalar
        def _(act):
            def place_dense(t):
                nc.scalar.activation(feats[:, :, :, 0].rearrange("p q s -> p s q"),
                                     dense_t[:, bass.ds(t * P, P)].rearrange("p (s q) -> p s q", s=SPG),
                                     ACT.Copy).then_inc(dense_placed, 1)

            def keep(t, j):
                act.wait_ge(turned, t * NB + j + 1)
                keep_batch(nc.scalar.copy, j).then_inc(kept, 1)

            def tile(t, ahead):
                for u in range(UNITS):
                    act.wait_ge(gram_done, t * UNITS + u + 1)
                    draw_block(nc.scalar.copy, u, 2)
                    draw_block(nc.scalar.copy, u, 3).then_inc(drawn_act, 1)
                todo = list(range(NB)) if ahead else []
                if ahead:
                    place_dense(t + 1)
                due = AHEAD[0] + AHEAD[1]
                for j in todo[:due]:
                    keep(t + 1, j)
                for c in range(C1):
                    act.wait_ge(h1_summed, t * C1 + c + 1)
                    nc.scalar.activation(h1[:, c, :], h1_sum[:, c, :], ACT.Relu).then_inc(h1_kept, 1)
                for j in todo[due:]:
                    keep(t + 1, j)

            act.wait_ge(dense_kept, 1)
            place_dense(0)
            act.wait_ge(columns_loaded, 16)
            for c in range(C1):
                act.wait_ge(l1_dense_done, c + 1)
                nc.scalar.activation(h1_dense[:, c, :], gram_ps[:, c, 0:B], ACT.Identity,
                                     bias=b1_sb[:, c:c + 1]).then_inc(h1_dense_kept, 1)
            for j in range(NB):
                keep(0, j)
            with act.Fori(0, TILES - 1) as t:
                tile(t, True)
            tile(TILES - 1, False)


TABLES = SLOTS - 1


def kernel(**inputs):
    import numpy as np
    import concourse.bacc as bacc
    from concourse.bass_utils import run_bass_kernel_spmd

    w1 = np.asarray(inputs["W_top1"])
    dense = np.asarray(inputs["r_dense_features"])
    ids = np.asarray(inputs["ids"])
    B, D = dense.shape
    sizes = [inputs[f"tbl_{i}"].shape[0] for i in range(TABLES)]
    looked = [i for i in range(TABLES) if sizes[i] == min(sizes)][:LOOKUPS]
    order = looked + [i for i in range(TABLES) if i not in looked]
    arrays = {"dense": dense, "gather_ids": ids[:, order[LOOKUPS:]], "look_ids": ids[:, looked].T}
    for i in range(TABLES):
        arrays[f"tbl_{i}"] = np.asarray(inputs[f"tbl_{i}"])
    arrays["w_dense_a"] = w1[:D]
    arrays["w_pairs"] = w1[pair_rows(D, order)]
    arrays["w_dense_b"] = w1[-D:]
    arrays["w2"] = np.asarray(inputs["W_top2"])
    arrays["columns"] = np.concatenate([np.asarray(inputs[name]).reshape(-1, P).T
                                        for name in ("b_top1", "b_top2", "W_top3")], axis=1)
    arrays = {name: np.ascontiguousarray(a) for name, a in arrays.items()}

    nc = bacc.Bacc("TRN2", target_bir_lowering=False, num_devices=1)
    aps = {name: nc.dram_tensor(name, a.shape, mybir.dt.from_np(a.dtype), kind="ExternalInput").ap()
           for name, a in arrays.items()}
    out = nc.dram_tensor("out", (B, 1), F32, kind="ExternalOutput").ap()
    tables = [aps[f"tbl_{i}"] for i in order]
    dlrm_tower(nc, aps["dense"], aps["gather_ids"], aps["look_ids"], tables[LOOKUPS:], tables[:LOOKUPS],
               aps["w_dense_a"], aps["w_pairs"], aps["w_dense_b"], aps["w2"], aps["columns"], out)
    result = run_bass_kernel_spmd(nc, [arrays], core_ids=[0])
    return result.results[0]["out"]
```

```python
from contextlib import ExitStack

import concourse.bass as bass
from concourse import mybir

F32 = mybir.dt.float32
F32R = mybir.dt.float32r
I32 = mybir.dt.int32
ALU = mybir.AluOpType
ACT = mybir.ActivationFunctionType

P = 128
SLOTS = 27
PAD = 32
SPG = P // PAD
GROUPS = P // SPG
BATCH = 4
BANK = 512
GPB = 4
UNIT = 2 * GPB
SPAN = SLOTS // 2 + 1
PAIRS = SLOTS * (SLOTS - 1) // 2
PAIR_TILES = [(a, min(a + P, PAIRS)) for a in range(0, PAIRS, P)]
LOOKUPS = 6
RING = 3
AHEAD = (2, 1, 1, 1)


def look_rows(vocabulary):
    return max(n for n in range(1, P + 1) if vocabulary % n == 0)


def pair_rows(dense_dim, order):
    def row(a, b):
        return dense_dim + a * (SLOTS - 1) - a * (a - 1) // 2 + b - a - 1

    feature = [0] + [f + 1 for f in order]
    rows = []
    for k in range(1, SPAN + 1):
        for c in range(SLOTS - 1):
            rows.append(row(*sorted(feature[s] for s in divmod(c * SLOTS + c + k, SLOTS))))
    return rows[:PAIRS]


def dlrm_tower(nc, dense, gather_ids, look_ids, gather_tables, look_tables,
               w_dense_a, w_pairs, w_dense_b, w2, columns, out):
    B, D = dense.shape
    F, L = len(gather_tables), len(look_tables)
    TILES = B // P
    N1, N2 = w2.shape
    C1, C2 = N1 // P, N2 // P
    LP = look_rows(look_tables[0].shape[0])
    LC = look_tables[0].shape[0] // LP
    BATCHES = [range(a, min(a + BATCH, F)) for a in range(0, F, BATCH)]
    NB = len(BATCHES)
    UNITS = GROUPS // UNIT
    assert D == P and L + F == SLOTS - 1

    with ExitStack() as ctx:
        def sb(name, shape, dt=F32):
            return ctx.enter_context(nc.sbuf_tensor(name, shape, dt))

        def psum(name, shape):
            return ctx.enter_context(nc.psum_tensor(name, shape, F32))

        def sem(name):
            return ctx.enter_context(nc.semaphore(name))

        ids_sb = sb("ids_sb", [P, TILES, F], I32)
        look_ids_sb = sb("look_ids_sb", [P, L, B], I32)
        look_sb = sb("look_sb", [LP, L, LC, D])
        row_of = sb("row_of", [LP, LC])
        look_hi = sb("look_hi", [LP, RING, LC, D], F32R)
        look_lo = sb("look_lo", [LP, RING, LC, D], F32R)
        one_hot = sb("one_hot", [LP, RING, LC, B], F32R)
        dense_sb = sb("dense_sb", [P, TILES, D])
        early = sb("early", [P, 1 + L, B])
        rows = sb("rows", [P, F, D])
        feats = sb("feats", [P, GROUPS, SPG, PAD])
        gram_sb = sb("gram_sb", [P, SLOTS, GROUPS])
        dots_pad = sb("dots_pad", [P, SLOTS + 1, PAD])
        dots = sb("dots", [P, (SLOTS + 1) * SLOTS])
        pairs = sb("pairs", [P, SPAN * (SLOTS - 1)])
        pairs_t = sb("pairs_t", [P, len(PAIR_TILES), P])
        h1 = sb("h1", [P, C1, P])
        h2 = sb("h2", [P, C2, P])
        y = sb("y", [1, B])
        ident = sb("ident", [P, P])
        wd_sb = sb("wd_sb", [P, 2, N1])
        wp_sb = sb("wp_sb", [P, len(PAIR_TILES), N1])
        w2_sb = sb("w2_sb", [P, C1, N2])
        columns_sb = sb("columns_sb", [P, C1 + 2 * C2])
        b1_sb, b2_sb, w3_sb = (columns_sb[:, a:b] for a, b in ((0, C1), (C1, C1 + C2), (C1 + C2, C1 + 2 * C2)))

        turn_ps = psum("turn_ps", [P, 2, BATCH, P])
        gram_ps = psum("gram_ps", [P, 2 * UNIT // GPB, BANK])
        pair_ps = psum("pair_ps", [P, BANK])
        l23_ps = psum("l23_ps", [P, BANK])

        def h1_ps(c):
            return gram_ps[:, c, 0:P]

        def h2_ps(m):
            return (pair_ps if m == 0 else l23_ps)[:, 0:P]

        assert C1 == 2 * UNIT // GPB and C2 == 2
        y_ps = l23_ps[0:1, P:2 * P]

        ids_loaded = sem("ids_loaded")
        look_ids_loaded = [sem(f"look_ids_loaded_{i}") for i in range(L)]
        dense_loaded = sem("dense_loaded")
        look_loaded = [sem(f"look_loaded_{i}") for i in range(L)]
        columns_loaded = sem("columns_loaded")
        weights_loaded = sem("weights_loaded")
        gathered = [sem(f"gathered_{f}") for f in range(F)]
        zeroed = sem("zeroed")
        ident_made = sem("ident_made")
        rows_numbered = sem("rows_numbered")
        pads_zeroed = sem("pads_zeroed")
        dense_turned = sem("dense_turned")
        dense_kept = sem("dense_kept")
        early_placed = sem("early_placed")
        hot_made = sem("hot_made")
        hi_made = sem("hi_made")
        lo_made = sem("lo_made")
        looked = sem("looked")
        look_kept = sem("look_kept")
        turned = sem("turned")
        kept = sem("kept")
        gram_done = sem("gram_done")
        drawn_dve = sem("drawn_dve")
        drawn_act = sem("drawn_act")
        dots_turned = sem("dots_turned")
        dots_packed = sem("dots_packed")
        pairs_packed = sem("pairs_packed")
        pairs_turned = sem("pairs_turned")
        pairs_kept = sem("pairs_kept")
        l1_done = sem("l1_done")
        h1_kept = sem("h1_kept")
        l2_done = sem("l2_done")
        h2_kept = sem("h2_kept")
        l3_done = sem("l3_done")
        y_kept = sem("y_kept")
        y_stored = sem("y_stored")

        def keep_batch(copy, j):
            first, n = 1 + L + BATCHES[j][0], len(BATCHES[j])
            src = turn_ps[:, j % 2, 0:n, :].rearrange("p f (s q) -> p s q f", s=SPG)
            return copy(feats[:, :, :, first:first + n].rearrange("p q s f -> p s q f"), src)

        def look_ps(i):
            return (pair_ps, l23_ps)[i % 2]

        def draw_block(copy, u, s):
            at = slice(s * PAD, (s + 1) * PAD)
            bank = (u % 2) * (UNIT // GPB)
            src = gram_ps[at, bank:bank + UNIT // GPB, 0:GPB * SPG * SLOTS].rearrange(
                "p h (l s c) -> p h l s c", l=GPB, s=SPG)[:, :, :, s, :]
            dst = gram_sb[at, :, u * UNIT:(u + 1) * UNIT].rearrange("p c (h l) -> p h l c", l=GPB)
            return copy(dst, src)

        block = ctx.enter_context(nc.Block())

        @block.sync
        def _(sp):
            sp.dma_start(ids_sb[:], gather_ids.rearrange("(t p) f -> p t f", p=P)).then_inc(ids_loaded, 16)
            for i in range(L):
                sp.dma_start(look_ids_sb[:, i, :], look_ids[i].partition_broadcast(P)).then_inc(look_ids_loaded[i], 16)
                sp.dma_start(look_sb[:, i, :, :].rearrange("p k d -> p (k d)"),
                             look_tables[i].rearrange("(p k) d -> p (k d)", k=LC)).then_inc(look_loaded[i], 16)
                if i == 0:
                    sp.dma_start(dense_sb[:], dense.rearrange("(t p) d -> p t d", p=P)).then_inc(dense_loaded, 16)
            sp.dma_start(wd_sb[:, 0, :], w_dense_a).then_inc(weights_loaded, 16)
            sp.dma_start(wd_sb[:, 1, :], w_dense_b).then_inc(weights_loaded, 16)
            sp.dma_start(columns_sb[:], columns).then_inc(columns_loaded, 16)
            for i, (a, b) in enumerate(PAIR_TILES):
                sp.dma_start(wp_sb[0:b - a, i, :], w_pairs[a:b, :]).then_inc(weights_loaded, 16)
            sp.dma_start(w2_sb[:], w2.rearrange("(c p) n -> p c n", p=P)).then_inc(weights_loaded, 16)
            sp.wait_ge(y_kept, TILES)
            sp.dma_start(out.rearrange("b o -> o b"), y[:]).then_inc(y_stored, 16)
            sp.wait_ge(y_stored, 16)

        WEIGHTS = 16 * (3 + len(PAIR_TILES))

        @block.gpsimd
        def _(pool):
            nc.gpsimd.memset(ident[:], 0.0).then_inc(zeroed, 1)
            nc.gpsimd.iota(row_of[:], [[1, LC]], base=0, channel_multiplier=LC,
                           allow_small_or_imprecise_dtypes=True).then_inc(rows_numbered, 1)
            pool.wait_ge(zeroed, 1)
            nc.gpsimd.affine_select(out=ident[:], in_=ident[:], compare_op=ALU.not_equal, fill=1.0, base=0,
                                    pattern=[[-1, P]], channel_multiplier=1).then_inc(ident_made, 1)
            pool.wait_ge(ids_loaded, 16)
            for t in range(TILES):
                for j, which in enumerate(BATCHES):
                    if t >= 1:
                        pool.wait_ge(turned, (t - 1) * NB + j + 1)
                    for f in which:
                        nc.gpsimd.indirect_dma_start(
                            out=rows[:, f, :], out_offset=None, in_=gather_tables[f],
                            in_offset=bass.IndirectOffsetOnAxis(ap=ids_sb[:, t, f:f + 1], axis=0)
                        ).then_inc(gathered[f], 16)

        @block.tensor
        def _(pe):
            def look_up(i):
                pe.wait_ge(hot_made, i + 1)
                pe.wait_ge(lo_made, i + 1)
                if i >= 2:
                    pe.wait_ge(look_kept, i - 1)
                for k in range(LC):
                    for part in (look_hi, look_lo):
                        last = nc.tensor.matmul(look_ps(i)[:, 0:B], part[:, i % RING, k, :],
                                                one_hot[:, i % RING, k, :], start=(k == 0 and part is look_hi),
                                                stop=(k == LC - 1 and part is look_lo))
                last.then_inc(looked, 1)

            def turn(t, j):
                if j >= 2:
                    pe.wait_ge(kept, t * NB + j - 1)
                for at, f in enumerate(BATCHES[j]):
                    pe.wait_ge(gathered[f], (t + 1) * 16)
                    last = nc.tensor.transpose(turn_ps[:, j % 2, at, :], rows[:, f, :], ident[:])
                last.then_inc(turned, 1)

            def gram(t):
                pe.wait_ge(kept, (t + 1) * NB)
                pe.wait_ge(early_placed, t + 1)
                for u in range(UNITS):
                    if u >= 2:
                        pe.wait_ge(drawn_dve, t * UNITS + u - 1)
                        pe.wait_ge(drawn_act, t * UNITS + u - 1)
                    for i in range(UNIT):
                        q = u * UNIT + i
                        at = i % GPB * SPG * SLOTS
                        dst = gram_ps[:, (u % 2) * (UNIT // GPB) + i // GPB, at:at + SPG * SLOTS]
                        last = nc.tensor.matmul(dst.rearrange("p (s c) -> p s c", s=SPG),
                                                feats[:, q, :, :].rearrange("p s c -> p (s c)"),
                                                feats[:, q, :, 0:SLOTS], start=True, stop=True)
                    last.then_inc(gram_done, 1)

            def layer1_dense(t):
                for c in range(C1):
                    drawn = t * UNITS + UNITS - 1 + c // (UNIT // GPB)
                    pe.wait_ge(drawn_dve, drawn)
                    pe.wait_ge(drawn_act, drawn)
                    for half in range(2):
                        nc.tensor.matmul(h1_ps(c), wd_sb[:, half, c * P:(c + 1) * P],
                                         early[:, 0, bass.ds(t * P, P)], start=(half == 0), stop=False)

            def turn_pairs(t):
                pe.wait_ge(pairs_packed, t + 1)
                for i, (a, b) in enumerate(PAIR_TILES):
                    last = nc.tensor.transpose(pair_ps[0:b - a, i * P:(i + 1) * P], pairs[:, a:b], ident[:])
                last.then_inc(pairs_turned, 1)

            def layer1_pairs(t):
                for c in range(C1):
                    for i, (a, b) in enumerate(PAIR_TILES):
                        pe.wait_ge(pairs_kept, t * 2 + (1 if b - a == P else 2))
                        last = nc.tensor.matmul(h1_ps(c), wp_sb[0:b - a, i, c * P:(c + 1) * P],
                                                pairs_t[0:b - a, i, :], start=False,
                                                stop=(i == len(PAIR_TILES) - 1))
                    last.then_inc(l1_done, 1)

            def layer2(t):
                for c in range(C1):
                    pe.wait_ge(h1_kept, t * C1 + c + 1)
                    for m in range(C2):
                        last = nc.tensor.matmul(h2_ps(m), w2_sb[:, c, m * P:(m + 1) * P], h1[:, c, :],
                                                start=(c == 0), stop=(c == C1 - 1))
                        if c == C1 - 1:
                            last.then_inc(l2_done, 1)

            def layer3(t):
                pe.wait_ge(h2_kept, (t + 1) * C2)
                for m in range(C2):
                    last = nc.tensor.matmul(y_ps, w3_sb[:, m:m + 1], h2[:, m, :], start=(m == 0), stop=(m == C2 - 1))
                last.then_inc(l3_done, 1)

            def tile(t, ahead):
                gram(t)
                layer1_dense(t)
                todo = list(range(NB)) if ahead else []
                for step, share in ((turn_pairs, AHEAD[0]), (layer1_pairs, AHEAD[1]), (layer2, AHEAD[2]),
                                    (layer3, AHEAD[3])):
                    for j in todo[:share]:
                        turn(t + 1, j)
                    todo = todo[share:]
                    step(t)
                for j in todo:
                    turn(t + 1, j)

            pe.wait_ge(ident_made, 1)
            pe.wait_ge(dense_loaded, 16)
            for t in range(TILES):
                last = nc.tensor.transpose(turn_ps[:, 1, t, :], dense_sb[:, t, :], ident[:])
            last.then_inc(dense_turned, 1)
            for i in range(L):
                look_up(i)
                if i == 0:
                    pe.wait_ge(dense_kept, 1)
                if i >= L - NB:
                    turn(0, i - (L - NB))
            for j in range(L, NB):
                turn(0, j)
            pe.wait_ge(weights_loaded, WEIGHTS)
            with pe.Fori(0, TILES - 1) as t:
                tile(t, True)
            tile(TILES - 1, False)

        @block.vector
        def _(dve):
            def make_hot(i):
                for k in range(LC):
                    last = nc.vector.tensor_scalar(one_hot[:, i % RING, k, :], look_ids_sb[0:LP, i, :],
                                                   row_of[:, k:k + 1], None, ALU.is_equal)
                last.then_inc(hot_made, 1)

            def tile(t):
                for u in range(UNITS):
                    dve.wait_ge(gram_done, t * UNITS + u + 1)
                    draw_block(nc.vector.tensor_copy, u, 0)
                    draw_block(nc.vector.tensor_copy, u, 1).then_inc(drawn_dve, 1)
                dve.wait_ge(drawn_dve, (t + 1) * UNITS)
                dve.wait_ge(drawn_act, (t + 1) * UNITS)
                nc.vector.transpose(dots_pad[:, 0:SLOTS, :].rearrange("p c f -> p (c f)"),
                                    gram_sb[:].rearrange("p c q -> p (c q)")).then_inc(dots_turned, 1)
                dve.wait_ge(dots_turned, t + 1)
                nc.vector.tensor_copy(dots[:].rearrange("p (c f) -> p c f", f=SLOTS),
                                      dots_pad[:, :, 0:SLOTS]).then_inc(dots_packed, 1)
                dve.wait_ge(dots_packed, t + 1)
                nc.vector.tensor_copy(pairs[:].rearrange("p (k c) -> p k c", k=SPAN),
                                      dots[:, 1:1 + (SLOTS - 1) * (SLOTS + 1)].rearrange(
                                          "p (c k) -> p k c", k=SLOTS + 1)[:, 0:SPAN, :]).then_inc(pairs_packed, 1)
                dve.wait_ge(pairs_turned, t + 1)
                whole = PAIRS // P
                nc.vector.tensor_copy(pairs_t[:, 0:whole, :],
                                      pair_ps[:, 0:whole * P].rearrange("p (i b) -> p i b", b=P)
                                      ).then_inc(pairs_kept, 1)
                rest = PAIRS - whole * P
                nc.vector.tensor_copy(pairs_t[0:rest, whole, :], pair_ps[0:rest, whole * P:(whole + 1) * P]
                                      ).then_inc(pairs_kept, 1)
                for c in range(C1):
                    dve.wait_ge(l1_done, t * C1 + c + 1)
                    nc.vector.tensor_scalar(h1[:, c, :], h1_ps(c), b1_sb[:, c:c + 1], 0.0,
                                            ALU.add, ALU.max).then_inc(h1_kept, 1)
                for m in range(C2):
                    dve.wait_ge(l2_done, t * C2 + m + 1)
                    nc.vector.tensor_scalar(h2[:, m, :], h2_ps(m), b2_sb[:, m:m + 1], 0.0,
                                            ALU.add, ALU.max).then_inc(h2_kept, 1)
                dve.wait_ge(l3_done, t + 1)
                nc.vector.tensor_copy(y[:, bass.ds(t * P, P)], y_ps).then_inc(y_kept, 1)

            nc.vector.memset(feats[:, :, :, SLOTS:PAD], 0.0).then_inc(pads_zeroed, 1)
            nc.vector.memset(dots_pad[:, SLOTS, :], 0.0).then_inc(pads_zeroed, 1)
            dve.wait_ge(pads_zeroed, 2)
            dve.wait_ge(rows_numbered, 1)
            for i in range(L):
                dve.wait_ge(look_ids_loaded[i], 16)
                if i >= RING:
                    dve.wait_ge(looked, i - RING + 1)
                make_hot(i)
                dve.wait_ge(hi_made, i + 1)
                nc.vector.tensor_tensor(look_lo[:, i % RING, :, :], look_sb[:, i, :, :],
                                        look_hi[:, i % RING, :, :].bitcast(F32), ALU.subtract).then_inc(lo_made, 1)
            dve.wait_ge(columns_loaded, 16)
            with dve.Fori(0, TILES - 1) as t:
                tile(t)
            tile(TILES - 1)

        @block.scalar
        def _(act):
            def make_hi(i):
                act.wait_ge(look_loaded[i], 16)
                if i >= RING:
                    act.wait_ge(looked, i - RING + 1)
                nc.scalar.copy(look_hi[:, i % RING, :, :], look_sb[:, i, :, :]).then_inc(hi_made, 1)

            def place_early(t):
                nc.scalar.copy(feats[:, :, :, 0:1 + L].rearrange("p q s f -> p s q f"),
                               early[:, :, bass.ds(t * P, P)].rearrange("p f (s q) -> p s q f", s=SPG)
                               ).then_inc(early_placed, 1)

            def keep(t, j):
                act.wait_ge(turned, t * NB + j + 1)
                keep_batch(nc.scalar.copy, j).then_inc(kept, 1)

            def tile(t, ahead):
                for u in range(UNITS):
                    act.wait_ge(gram_done, t * UNITS + u + 1)
                    draw_block(nc.scalar.copy, u, 2)
                    draw_block(nc.scalar.copy, u, 3).then_inc(drawn_act, 1)
                todo = list(range(NB)) if ahead else []
                if ahead:
                    place_early(t + 1)
                for j in todo:
                    keep(t + 1, j)

            make_hi(0)
            act.wait_ge(dense_turned, 1)
            nc.scalar.copy(early[:, 0, :].rearrange("p (t b) -> p t b", b=P), turn_ps[:, 1, :, :]).then_inc(dense_kept, 1)
            make_hi(1)
            for i in range(L):
                if i + 2 < L:
                    make_hi(i + 2)
                act.wait_ge(looked, i + 1)
                nc.scalar.copy(early[:, 1 + i, :], look_ps(i)[:, 0:B]).then_inc(look_kept, 1)
                if i >= L - NB:
                    keep(0, i - (L - NB))
            act.wait_ge(dense_kept, 1)
            act.wait_ge(look_kept, L)
            place_early(0)
            with act.Fori(0, TILES - 1) as t:
                tile(t, True)
            tile(TILES - 1, False)


TABLES = SLOTS - 1


def kernel(**inputs):
    import numpy as np
    import concourse.bacc as bacc
    from concourse.bass_utils import run_bass_kernel_spmd

    w1 = np.asarray(inputs["W_top1"])
    dense = np.asarray(inputs["r_dense_features"])
    ids = np.asarray(inputs["ids"])
    B, D = dense.shape
    sizes = [inputs[f"tbl_{i}"].shape[0] for i in range(TABLES)]
    looked = [i for i in range(TABLES) if sizes[i] == min(sizes)][:LOOKUPS]
    order = looked + [i for i in range(TABLES) if i not in looked]
    arrays = {"dense": dense, "gather_ids": ids[:, order[LOOKUPS:]], "look_ids": ids[:, looked].T}
    for i in range(TABLES):
        arrays[f"tbl_{i}"] = np.asarray(inputs[f"tbl_{i}"])
    arrays["w_dense_a"] = w1[:D]
    arrays["w_pairs"] = w1[pair_rows(D, order)]
    arrays["w_dense_b"] = w1[-D:]
    arrays["w2"] = np.asarray(inputs["W_top2"])
    arrays["columns"] = np.concatenate([np.asarray(inputs[name]).reshape(-1, P).T
                                        for name in ("b_top1", "b_top2", "W_top3")], axis=1)
    arrays = {name: np.ascontiguousarray(a) for name, a in arrays.items()}

    nc = bacc.Bacc("TRN2", target_bir_lowering=False, num_devices=1)
    aps = {name: nc.dram_tensor(name, a.shape, mybir.dt.from_np(a.dtype), kind="ExternalInput").ap()
           for name, a in arrays.items()}
    out = nc.dram_tensor("out", (B, 1), F32, kind="ExternalOutput").ap()
    tables = [aps[f"tbl_{i}"] for i in order]
    dlrm_tower(nc, aps["dense"], aps["gather_ids"], aps["look_ids"], tables[LOOKUPS:], tables[:LOOKUPS],
               aps["w_dense_a"], aps["w_pairs"], aps["w_dense_b"], aps["w2"], aps["columns"], out)
    result = run_bass_kernel_spmd(nc, [arrays], core_ids=[0])
    return result.results[0]["out"]
```

```python
from contextlib import ExitStack

import concourse.bass as bass
from concourse import mybir

F32 = mybir.dt.float32
F32R = mybir.dt.float32r
I32 = mybir.dt.int32
ALU = mybir.AluOpType
ACT = mybir.ActivationFunctionType

P = 128
SLOTS = 27
PAD = 32
SPG = P // PAD
GROUPS = P // SPG
BATCH = 4
BANK = 512
GPB = 4
UNIT = 2 * GPB
SPAN = SLOTS // 2 + 1
PAIRS = SLOTS * (SLOTS - 1) // 2
PAIR_TILES = [(a, min(a + P, PAIRS)) for a in range(0, PAIRS, P)]
EARLY = 5
LATE = 3
LATE_FROM = 2
LATE_AT = ((0, 1), (0, 3), (1, 1))
LOOKUPS = EARLY + LATE
RING = 3
HOTS = 3
LOADED = 5
AHEAD = ((1, 1, 1, 1, 2), (1, 1, 1, 1, 1), (1, 1, 1, 1, 1))
WARM = 26
SPLIT_BEFORE = EARLY + 2
BEHIND = 1
GAP_CHUNKS = (4, 4)


def look_rows(vocabulary):
    return max(n for n in range(1, P + 1) if vocabulary % n == 0)


def pair_rows(dense_dim, order):
    def row(a, b):
        return dense_dim + a * (SLOTS - 1) - a * (a - 1) // 2 + b - a - 1

    feature = [0] + [f + 1 for f in order]
    rows = []
    for k in range(1, SPAN + 1):
        for c in range(SLOTS - 1):
            rows.append(row(*sorted(feature[s] for s in divmod(c * SLOTS + c + k, SLOTS))))
    return rows[:PAIRS]


def looked_slots(t):
    return EARLY if t < LATE_FROM else LOOKUPS


def dlrm_tower(nc, dense, ids, look_ids, tables, w_dense_a, w_pairs, w_dense_b, w2, columns, out):
    B, D = dense.shape
    L, T = LOOKUPS, len(tables)
    F = T - EARLY
    TILES = B // P
    N1, N2 = w2.shape
    C1, C2 = N1 // P, N2 // P
    LP = look_rows(tables[0].shape[0])
    LC = tables[0].shape[0] // LP
    BATCHES = [[range(a, min(a + BATCH, T)) for a in range(looked_slots(t), T, BATCH)] for t in range(TILES)]
    UNITS = GROUPS // UNIT
    assert D == P and T == SLOTS - 1

    def batches_before(t, j=0):
        return sum(len(b) for b in BATCHES[:t]) + j

    with ExitStack() as ctx:
        def sb(name, shape, dt=F32):
            return ctx.enter_context(nc.sbuf_tensor(name, shape, dt))

        def psum(name, shape):
            return ctx.enter_context(nc.psum_tensor(name, shape, F32))

        def sem(name):
            return ctx.enter_context(nc.semaphore(name))

        ids_sb = sb("ids_sb", [P, TILES, T], I32)
        look_ids_sb = sb("look_ids_sb", [P, L, B], I32)
        look_sb = sb("look_sb", [LP, LOADED, LC, D])
        row_of = sb("row_of", [LP, LC])
        minus_row = sb("minus_row", [LP, LC])
        look_hi = sb("look_hi", [LP, RING, LC, D], F32R)
        look_lo = sb("look_lo", [LP, RING, LC, D], F32R)
        distance = sb("distance", [LP, B])
        one_hot = sb("one_hot", [LP, HOTS, LC, B], F32R)
        dense_sb = sb("dense_sb", [P, TILES, D])
        early = sb("early", [P, 1 + L, B])
        rows = sb("rows", [P, 2, F, D])
        feats = sb("feats", [P, GROUPS, SPG, PAD])
        gram_sb = sb("gram_sb", [P, SLOTS, GROUPS])
        dots_pad = sb("dots_pad", [P, SLOTS + 1, PAD])
        dots = sb("dots", [P, (SLOTS + 1) * SLOTS])
        pairs = sb("pairs", [P, SPAN * (SLOTS - 1)])
        pairs_t = sb("pairs_t", [P, len(PAIR_TILES), P])
        h1 = sb("h1", [P, C1, P])
        h2 = sb("h2", [P, C2, P])
        y = sb("y", [1, B])
        ident = sb("ident", [P, P])
        wd_sb = sb("wd_sb", [P, 2, N1])
        wd_sum = sb("wd_sum", [P, N1])
        wp_sb = sb("wp_sb", [P, len(PAIR_TILES), N1])
        w2_sb = sb("w2_sb", [P, C1, N2])
        columns_sb = sb("columns_sb", [P, C1 + 2 * C2])
        b1_sb, b2_sb, w3_sb = (columns_sb[:, a:b] for a, b in ((0, C1), (C1, C1 + C2), (C1 + C2, C1 + 2 * C2)))

        turn_ps = psum("turn_ps", [P, 2, BATCH, P])
        gram_ps = psum("gram_ps", [P, 2 * UNIT // GPB, BANK])
        pair_ps = psum("pair_ps", [P, BANK])
        look_ps = psum("look_ps", [P, BANK])

        def h1_ps(c):
            return gram_ps[:, c, 0:P]

        def h2_ps(m):
            return (pair_ps if m == 0 else look_ps)[:, 0:P]

        assert C1 == 2 * UNIT // GPB and C2 == 2
        y_ps = pair_ps[0:1, P:2 * P]

        ids_loaded = sem("ids_loaded")
        look_ids_loaded = [sem(f"look_ids_loaded_{i}") for i in range(L)]
        dense_loaded = sem("dense_loaded")
        look_loaded = [sem(f"look_loaded_{i}") for i in range(L)]
        columns_loaded = sem("columns_loaded")
        dense_weights_loaded = sem("dense_weights_loaded")
        wd_summed = sem("wd_summed")
        weights_loaded = sem("weights_loaded")
        gathered = [sem(f"gathered_{f}") for f in range(F)]
        zeroed = sem("zeroed")
        ident_made = sem("ident_made")
        rows_numbered = sem("rows_numbered")
        rows_negated = sem("rows_negated")
        pads_zeroed = sem("pads_zeroed")
        dense_turned = sem("dense_turned")
        dense_kept = sem("dense_kept")
        early_placed = sem("early_placed")
        hot_made = sem("hot_made")
        distance_made = sem("distance_made")
        last_hot_made = sem("last_hot_made")
        hi_made = sem("hi_made")
        lo_made = sem("lo_made")
        looked = sem("looked")
        look_kept = sem("look_kept")
        turned = sem("turned")
        kept = sem("kept")
        gram_done = sem("gram_done")
        drawn_dve = sem("drawn_dve")
        drawn_act = sem("drawn_act")
        dots_turned = sem("dots_turned")
        dots_packed = sem("dots_packed")
        pairs_packed = sem("pairs_packed")
        pairs_turned = sem("pairs_turned")
        pairs_kept = sem("pairs_kept")
        l1_done = sem("l1_done")
        h1_kept = sem("h1_kept")
        l2_done = sem("l2_done")
        h2_kept = [sem(f"h2_kept_{m}") for m in range(C2)]
        l3_done = sem("l3_done")
        y_kept = sem("y_kept")
        y_stored = sem("y_stored")

        def turn_bank(t, j):
            return batches_before(t, j) % 2

        def keep_batch(copy, t, j):
            first, n = 1 + BATCHES[t][j][0], len(BATCHES[t][j])
            src = turn_ps[:, turn_bank(t, j), 0:n, :].rearrange("p f (s q) -> p s q f", s=SPG)
            return copy(feats[:, :, :, first:first + n].rearrange("p q s f -> p s q f"), src)

        def look_samples(i):
            return slice(0 if i < EARLY else LATE_FROM * P, B)

        def look_bank(i):
            samples = look_samples(i)
            bank = pair_ps if i < EARLY and i % 2 else look_ps
            return bank[:, 0:samples.stop - samples.start]

        def between(t, step):
            if t == TILES - 1:
                return [], []
            begin, n = sum(AHEAD[t][:step]), len(BATCHES[t + 1])
            end = begin + AHEAD[t][step] if step < len(AHEAD[t]) else n
            return [EARLY + e for e, at in enumerate(LATE_AT) if at == (t, step)], range(min(begin, n), min(end, n))

        def draw_block(copy, u, s):
            at = slice(s * PAD, (s + 1) * PAD)
            bank = (u % 2) * (UNIT // GPB)
            src = gram_ps[at, bank:bank + UNIT // GPB, 0:GPB * SPG * SLOTS].rearrange(
                "p h (l s c) -> p h l s c", l=GPB, s=SPG)[:, :, :, s, :]
            dst = gram_sb[at, :, u * UNIT:(u + 1) * UNIT].rearrange("p c (h l) -> p h l c", l=GPB)
            return copy(dst, src)

        def first_turned_after(i):
            n = len(BATCHES[0])
            skip = max(EARLY - n, BEHIND)
            return range(max(i - skip, 0), n if i == EARLY - 1 else max(i + 1 - skip, 0))

        block = ctx.enter_context(nc.Block())

        @block.sync
        def _(sp):
            sp.dma_start(ids_sb[:], ids.rearrange("(t p) f -> p t f", p=P)).then_inc(ids_loaded, 16)
            for i in range(L):
                sp.dma_start(look_ids_sb[:, i, :], look_ids[i].partition_broadcast(P)).then_inc(look_ids_loaded[i], 16)
                if i == SPLIT_BEFORE:
                    sp.wait_ge(gathered[F - 1], 16)
                if i >= LOADED:
                    sp.wait_ge(lo_made, i - LOADED + 1)
                sp.dma_start(look_sb[:, i % LOADED, :, :].rearrange("p k d -> p (k d)"),
                             tables[i].rearrange("(p k) d -> p (k d)", k=LC)).then_inc(look_loaded[i], 16)
                if i == 0:
                    sp.dma_start(dense_sb[:], dense.rearrange("(t p) d -> p t d", p=P)).then_inc(dense_loaded, 16)
                if i == EARLY - 1:
                    sp.dma_start(wd_sb[:, 0, :], w_dense_a).then_inc(dense_weights_loaded, 16)
                    sp.dma_start(wd_sb[:, 1, :], w_dense_b).then_inc(dense_weights_loaded, 16)
                    sp.dma_start(columns_sb[:], columns).then_inc(columns_loaded, 16)
            for i, (a, b) in enumerate(PAIR_TILES):
                sp.dma_start(wp_sb[0:b - a, i, :], w_pairs[a:b, :]).then_inc(weights_loaded, 16)
            sp.dma_start(w2_sb[:], w2.rearrange("(c p) n -> p c n", p=P)).then_inc(weights_loaded, 16)
            sp.wait_ge(y_kept, TILES)
            sp.dma_start(out.rearrange("b o -> o b"), y[:]).then_inc(y_stored, 16)
            sp.wait_ge(y_stored, 16)

        WEIGHTS = 16 * (1 + len(PAIR_TILES))

        @block.gpsimd
        def _(pool):
            nc.gpsimd.memset(ident[:], 0.0).then_inc(zeroed, 1)
            nc.gpsimd.iota(row_of[:], [[1, LC]], base=0, channel_multiplier=LC,
                           allow_small_or_imprecise_dtypes=True).then_inc(rows_numbered, 1)
            pool.wait_ge(zeroed, 1)
            nc.gpsimd.affine_select(out=ident[:], in_=ident[:], compare_op=ALU.not_equal, fill=1.0, base=0,
                                    pattern=[[-1, P]], channel_multiplier=1).then_inc(ident_made, 1)
            pool.wait_ge(ids_loaded, 16)
            for t in range(TILES):
                for j, which in enumerate(BATCHES[t]):
                    for f in which:
                        if t >= 1:
                            pool.wait_ge(gathered[f - EARLY], t * 16)
                        if t >= 2:
                            pool.wait_ge(turned, batches_before(t - 2, (f - looked_slots(t - 2)) // BATCH) + 1)
                        nc.gpsimd.indirect_dma_start(
                            out=rows[:, t % 2, f - EARLY, :], out_offset=None, in_=tables[f],
                            in_offset=bass.IndirectOffsetOnAxis(ap=ids_sb[:, t, f:f + 1], axis=0)
                        ).then_inc(gathered[f - EARLY], 16)

        @block.tensor
        def _(pe):
            def look_up(i):
                pe.wait_ge(hot_made, i + 1)
                if i < EARLY:
                    pe.wait_ge(last_hot_made, i + 1)
                pe.wait_ge(lo_made, i + 1)
                if i >= EARLY:
                    pe.wait_ge(look_kept, i)
                elif i >= 2:
                    pe.wait_ge(look_kept, i - 1)
                for k in range(LC):
                    for part in (look_hi, look_lo):
                        last = nc.tensor.matmul(look_bank(i), part[:, i % RING, k, :],
                                                one_hot[:, i % HOTS, k, look_samples(i)],
                                                start=(k == 0 and part is look_hi),
                                                stop=(k == LC - 1 and part is look_lo))
                last.then_inc(looked, 1)

            def turn(t, j):
                if batches_before(t, j) >= 2:
                    pe.wait_ge(kept, batches_before(t, j) - 1)
                for at, f in enumerate(BATCHES[t][j]):
                    pe.wait_ge(gathered[f - EARLY], (t + 1) * 16)
                    last = nc.tensor.transpose(turn_ps[:, turn_bank(t, j), at, :], rows[:, t % 2, f - EARLY, :],
                                               ident[:])
                last.then_inc(turned, 1)

            def gram(t):
                pe.wait_ge(kept, batches_before(t + 1))
                pe.wait_ge(early_placed, t + 1)
                for u in range(UNITS):
                    if u >= 2:
                        pe.wait_ge(drawn_dve, t * UNITS + u - 1)
                        pe.wait_ge(drawn_act, t * UNITS + u - 1)
                    for i in range(UNIT):
                        q = u * UNIT + i
                        at = i % GPB * SPG * SLOTS
                        dst = gram_ps[:, (u % 2) * (UNIT // GPB) + i // GPB, at:at + SPG * SLOTS]
                        last = nc.tensor.matmul(dst.rearrange("p (s c) -> p s c", s=SPG),
                                                feats[:, q, :, :].rearrange("p s c -> p (s c)"),
                                                feats[:, q, :, 0:SLOTS], start=True, stop=True)
                    last.then_inc(gram_done, 1)

            def layer1_dense(t, half):
                for c in range(half * C1 // 2, (half + 1) * C1 // 2):
                    drawn = t * UNITS + UNITS - 1 + c // (UNIT // GPB)
                    pe.wait_ge(drawn_dve, drawn)
                    pe.wait_ge(drawn_act, drawn)
                    nc.tensor.matmul(h1_ps(c), wd_sum[:, c * P:(c + 1) * P], early[:, 0, bass.ds(t * P, P)],
                                     start=True, stop=False)

            def turn_pairs(t):
                pe.wait_ge(pairs_packed, t + 1)
                for i, (a, b) in enumerate(PAIR_TILES):
                    last = nc.tensor.transpose(pair_ps[0:b - a, i * P:(i + 1) * P], pairs[:, a:b], ident[:])
                last.then_inc(pairs_turned, 1)

            def layer1_pairs(t):
                if t == 0:
                    pe.wait_ge(weights_loaded, WEIGHTS)
                for c in range(C1):
                    for i, (a, b) in enumerate(PAIR_TILES):
                        pe.wait_ge(pairs_kept, t * 2 + (1 if b - a == P else 2))
                        last = nc.tensor.matmul(h1_ps(c), wp_sb[0:b - a, i, c * P:(c + 1) * P],
                                                pairs_t[0:b - a, i, :], start=False,
                                                stop=(i == len(PAIR_TILES) - 1))
                    last.then_inc(l1_done, 1)

            def layer2(t):
                pe.wait_ge(look_kept, EARLY + sum(at <= (t, 3) for at in LATE_AT))
                for m in range(C2):
                    for c in range(C1):
                        if m == 0:
                            pe.wait_ge(h1_kept, t * C1 + c + 1)
                        last = nc.tensor.matmul(h2_ps(m), w2_sb[:, c, m * P:(m + 1) * P], h1[:, c, :],
                                                start=(c == 0), stop=(c == C1 - 1))
                    last.then_inc(l2_done, 1)

            def layer3(t):
                for m in range(C2):
                    pe.wait_ge(h2_kept[m], t + 1)
                    last = nc.tensor.matmul(y_ps, w3_sb[:, m:m + 1], h2[:, m, :], start=(m == 0), stop=(m == C2 - 1))
                last.then_inc(l3_done, 1)

            def ahead(t, step):
                late, batches = between(t, step)
                for i in late:
                    look_up(i)
                for j in batches:
                    turn(t + 1, j)

            pe.wait_ge(ident_made, 1)
            for _ in range(WARM):
                nc.tensor.transpose(pair_ps[:, 0:P], ident[:], ident[:])
            pe.wait_ge(dense_loaded, 16)
            for t in range(TILES):
                last = nc.tensor.transpose(turn_ps[:, 1, t, :], dense_sb[:, t, :], ident[:])
            last.then_inc(dense_turned, 1)
            for i in range(EARLY):
                look_up(i)
                if i == 0:
                    pe.wait_ge(dense_kept, 1)
                for j in first_turned_after(i):
                    turn(0, j)
            for t in range(TILES):
                gram(t)
                if t == 0:
                    pe.wait_ge(wd_summed, 1)
                layer1_dense(t, 0)
                ahead(t, 0)
                layer1_dense(t, 1)
                for step, do in enumerate((turn_pairs, layer1_pairs, layer2, layer3)):
                    ahead(t, 1 + step)
                    do(t)
                ahead(t, 5)

        @block.vector
        def _(dve):
            def make_hot(i, chunks=range(LC)):
                samples = look_samples(i)
                if chunks[0] == 0:
                    dve.wait_ge(look_ids_loaded[i], 16)
                    if i >= HOTS:
                        dve.wait_ge(looked, i - HOTS + 1)
                for k in chunks:
                    last = nc.vector.tensor_scalar(one_hot[:, i % HOTS, k, samples], look_ids_sb[0:LP, i, samples],
                                                   row_of[:, k:k + 1], None, ALU.is_equal)
                if chunks[-1] == (LC - 2 if i < EARLY else LC - 1):
                    last.then_inc(hot_made, 1)

            def make_lo(i):
                dve.wait_ge(hi_made, i + 1)
                nc.vector.tensor_tensor(look_lo[:, i % RING, :, :], look_sb[:, i % LOADED, :, :],
                                        look_hi[:, i % RING, :, :].bitcast(F32), ALU.subtract).then_inc(lo_made, 1)

            def tile(t):
                late = [i for i in range(SPLIT_BEFORE, L) if i == SPLIT_BEFORE + t]
                for u in range(UNITS):
                    dve.wait_ge(gram_done, t * UNITS + u + 1)
                    draw_block(nc.vector.tensor_copy, u, 0)
                    draw_block(nc.vector.tensor_copy, u, 1).then_inc(drawn_dve, 1)
                    for i in late:
                        if u < len(GAP_CHUNKS):
                            begin = sum(GAP_CHUNKS[:u])
                            make_hot(i, range(begin, begin + GAP_CHUNKS[u]))
                        elif u == len(GAP_CHUNKS):
                            make_lo(i)
                dve.wait_ge(drawn_dve, (t + 1) * UNITS)
                dve.wait_ge(drawn_act, (t + 1) * UNITS)
                nc.vector.transpose(dots_pad[:, 0:SLOTS, :].rearrange("p c f -> p (c f)"),
                                    gram_sb[:].rearrange("p c q -> p (c q)")).then_inc(dots_turned, 1)
                dve.wait_ge(dots_turned, t + 1)
                nc.vector.tensor_copy(dots[:].rearrange("p (c f) -> p c f", f=SLOTS),
                                      dots_pad[:, :, 0:SLOTS]).then_inc(dots_packed, 1)
                dve.wait_ge(dots_packed, t + 1)
                nc.vector.tensor_copy(pairs[:].rearrange("p (k c) -> p k c", k=SPAN),
                                      dots[:, 1:1 + (SLOTS - 1) * (SLOTS + 1)].rearrange(
                                          "p (c k) -> p k c", k=SLOTS + 1)[:, 0:SPAN, :]).then_inc(pairs_packed, 1)
                dve.wait_ge(pairs_turned, t + 1)
                whole = PAIRS // P
                nc.vector.tensor_copy(pairs_t[:, 0:whole, :],
                                      pair_ps[:, 0:whole * P].rearrange("p (i b) -> p i b", b=P)
                                      ).then_inc(pairs_kept, 1)
                rest = PAIRS - whole * P
                nc.vector.tensor_copy(pairs_t[0:rest, whole, :], pair_ps[0:rest, whole * P:(whole + 1) * P]
                                      ).then_inc(pairs_kept, 1)
                for c in range(C1):
                    dve.wait_ge(l1_done, t * C1 + c + 1)
                    nc.vector.tensor_scalar(h1[:, c, :], h1_ps(c), b1_sb[:, c:c + 1], 0.0,
                                            ALU.add, ALU.max).then_inc(h1_kept, 1)
                dve.wait_ge(l2_done, t * C2 + 1)
                nc.vector.tensor_scalar(h2[:, 0, :], h2_ps(0), b2_sb[:, 0:1], 0.0, ALU.add, ALU.max).then_inc(h2_kept[0], 1)
                dve.wait_ge(l3_done, t + 1)
                nc.vector.tensor_copy(y[:, bass.ds(t * P, P)], y_ps).then_inc(y_kept, 1)

            nc.vector.memset(feats[:, :, :, SLOTS:PAD], 0.0).then_inc(pads_zeroed, 1)
            nc.vector.memset(dots_pad[:, SLOTS, :], 0.0).then_inc(pads_zeroed, 1)
            dve.wait_ge(pads_zeroed, 2)
            dve.wait_ge(rows_numbered, 1)
            for i in range(SPLIT_BEFORE):
                make_hot(i, range(LC - 1 if i < EARLY else LC))
                make_lo(i)
            dve.wait_ge(dense_weights_loaded, 32)
            nc.vector.tensor_tensor(wd_sum[:], wd_sb[:, 0, :], wd_sb[:, 1, :], ALU.add).then_inc(wd_summed, 1)
            dve.wait_ge(columns_loaded, 16)
            for t in range(TILES):
                tile(t)

        @block.scalar
        def _(act):
            def make_hi(i):
                act.wait_ge(look_loaded[i], 16)
                if i >= RING:
                    act.wait_ge(looked, i - RING + 1)
                nc.scalar.copy(look_hi[:, i % RING, :, :], look_sb[:, i % LOADED, :, :]).then_inc(hi_made, 1)

            def make_last_hot(i):
                act.wait_ge(look_ids_loaded[i], 16)
                if i >= HOTS:
                    act.wait_ge(looked, i - HOTS + 1)
                if i >= 1:
                    act.wait_ge(last_hot_made, i)
                nc.scalar.activation(distance[:], look_ids_sb[0:LP, i, :], ACT.Abs,
                                     bias=minus_row[:, LC - 1:LC]).then_inc(distance_made, 1)
                act.wait_ge(distance_made, i + 1)
                nc.scalar.activation(one_hot[:, i % HOTS, LC - 1, :], distance[:], ACT.Relu,
                                     bias=1.0, scale=-1.0).then_inc(last_hot_made, 1)

            def keep_look(i):
                act.wait_ge(looked, i + 1)
                nc.scalar.copy(early[:, 1 + i, look_samples(i)], look_bank(i)).then_inc(look_kept, 1)

            def place_early(t):
                n = 1 + looked_slots(t)
                act.wait_ge(look_kept, looked_slots(t))
                nc.scalar.copy(feats[:, :, :, 0:n].rearrange("p q s f -> p s q f"),
                               early[:, 0:n, t * P:(t + 1) * P].rearrange("p f (s q) -> p s q f", s=SPG)
                               ).then_inc(early_placed, 1)

            def keep(t, j):
                act.wait_ge(turned, batches_before(t, j) + 1)
                keep_batch(nc.scalar.copy, t, j).then_inc(kept, 1)

            act.wait_ge(rows_numbered, 1)
            nc.scalar.activation(minus_row[:], row_of[:], ACT.Copy, scale=-1.0).then_inc(rows_negated, 1)
            act.wait_ge(rows_negated, 1)
            make_hi(0)
            make_last_hot(0)
            act.wait_ge(dense_turned, 1)
            nc.scalar.copy(early[:, 0, :].rearrange("p (t b) -> p t b", b=P), turn_ps[:, 1, :, :]).then_inc(dense_kept, 1)
            make_hi(1)
            make_last_hot(1)
            for i in range(EARLY):
                if i + 2 <= EARLY:
                    make_hi(i + 2)
                if i + 2 < EARLY:
                    make_last_hot(i + 2)
                keep_look(i)
                if i == EARLY - 1:
                    act.wait_ge(dense_kept, 1)
                    place_early(0)
                for j in first_turned_after(i):
                    keep(0, j)
            for i in range(EARLY + 1, SPLIT_BEFORE):
                make_hi(i)
            act.wait_ge(columns_loaded, 16)
            for t in range(TILES):
                for u in range(UNITS):
                    act.wait_ge(gram_done, t * UNITS + u + 1)
                    draw_block(nc.scalar.copy, u, 2)
                    draw_block(nc.scalar.copy, u, 3).then_inc(drawn_act, 1)
                    if u == 0 and SPLIT_BEFORE + t < L:
                        make_hi(SPLIT_BEFORE + t)
                for step in range(6):
                    if step == 4:
                        act.wait_ge(l2_done, (t + 1) * C2)
                        nc.scalar.activation(h2[:, 1, :], h2_ps(1), ACT.Relu, bias=b2_sb[:, 1:2]).then_inc(h2_kept[1], 1)
                    late, batches = between(t, step)
                    for i in late:
                        keep_look(i)
                    for j in batches:
                        keep(t + 1, j)
                    if step == max([1] + [at[1] for at in LATE_AT if at[0] == t]) and t + 1 < TILES:
                        place_early(t + 1)


TABLES = SLOTS - 1


def kernel(**inputs):
    import numpy as np
    import concourse.bacc as bacc
    from concourse.bass_utils import run_bass_kernel_spmd

    w1 = np.asarray(inputs["W_top1"])
    dense = np.asarray(inputs["r_dense_features"])
    ids = np.asarray(inputs["ids"])
    B, D = dense.shape
    sizes = [inputs[f"tbl_{i}"].shape[0] for i in range(TABLES)]
    looked = [i for i in range(TABLES) if sizes[i] == min(sizes)][:LOOKUPS]
    order = looked + [i for i in range(TABLES) if i not in looked]
    arrays = {"dense": dense, "ids": ids[:, order], "look_ids": ids[:, looked].T}
    for i in range(TABLES):
        arrays[f"tbl_{i}"] = np.asarray(inputs[f"tbl_{i}"])
    arrays["w_dense_a"] = w1[:D]
    arrays["w_pairs"] = w1[pair_rows(D, order)]
    arrays["w_dense_b"] = w1[-D:]
    arrays["w2"] = np.asarray(inputs["W_top2"])
    arrays["columns"] = np.concatenate([np.asarray(inputs[name]).reshape(-1, P).T
                                        for name in ("b_top1", "b_top2", "W_top3")], axis=1)
    arrays = {name: np.ascontiguousarray(a) for name, a in arrays.items()}

    nc = bacc.Bacc("TRN2", target_bir_lowering=False, num_devices=1)
    aps = {name: nc.dram_tensor(name, a.shape, mybir.dt.from_np(a.dtype), kind="ExternalInput").ap()
           for name, a in arrays.items()}
    out = nc.dram_tensor("out", (B, 1), F32, kind="ExternalOutput").ap()
    dlrm_tower(nc, aps["dense"], aps["ids"], aps["look_ids"], [aps[f"tbl_{i}"] for i in order],
               aps["w_dense_a"], aps["w_pairs"], aps["w_dense_b"], aps["w2"], aps["columns"], out)
    result = run_bass_kernel_spmd(nc, [arrays], core_ids=[0])
    return result.results[0]["out"]
```
